# Optimizing a Trainium2 kernel written in Bass

```python
import numpy as np
import jax
import jax.numpy as jnp

def _softmax(x, axis=-1):
    return jax.nn.softmax(x, axis=axis)

def _gelu(x):
    return jax.nn.gelu(x, approximate=True)

def _silu(x):
    return jax.nn.silu(x)

def _sigmoid(x):
    return jax.nn.sigmoid(x)

def _layernorm(x, axis=-1, eps=1e-05):
    m = jnp.mean(x, axis=axis, keepdims=True)
    v = jnp.var(x, axis=axis, keepdims=True)
    return (x - m) / jnp.sqrt(v + eps)

def _scatter_add(tgt, idx, src, axis=0):
    return tgt.at[idx].add(src)

def _segment_sum(src, seg, n):
    return jax.ops.segment_sum(src, seg, n)
kernel_name = 'mk_adj_resnorm_d1_adj_r2_607cfe'

def setup_inputs(seed: int=0):
    np.random.seed(seed)
    _w = jnp.asarray

    def _rec_inputs():
        import jax
        import jax.numpy as jnp
        _gk = jax.random.key(seed)
        x = -0.0002928 + 1 * jax.random.normal(jax.random.fold_in(_gk, 1), (16, 512, 256), jnp.float32)
        _a = jax.random.bernoulli(jax.random.fold_in(_gk, 2), 0.0078125, (16, 512, 512))
        _a = jnp.logical_or(_a, jnp.eye(512, dtype=bool))
        adj = _a.astype(jnp.int32)
        return (x, adj)
    x, adj = _rec_inputs()

    def _L0_gnn_setup():
        import jax, jax.numpy as jnp
        import numpy as np
        B, N, D = (8, 512, 256)
        NH = 8
        DK = D // NH
        key = jax.random.key(seed)
        ks = jax.random.split(key, 6)
        x = jax.random.normal(ks[0], (B, N, D), dtype=jnp.float32)
        adj = jax.random.randint(ks[1], (B, N, N), 0, 2, dtype=jnp.int32)
        adj = jnp.maximum(adj, jnp.eye(N, dtype=jnp.int32)[None])
        s = 1.0 / np.sqrt(D)
        Wq = jax.random.normal(ks[2], (D, D), dtype=jnp.float32) * s
        Wk = jax.random.normal(ks[3], (D, D), dtype=jnp.float32) * s
        Wv = jax.random.normal(ks[4], (D, D), dtype=jnp.float32) * s
        Wo = jax.random.normal(ks[5], (D, D), dtype=jnp.float32) * s
        return {'x': x, 'adj': adj, 'Wq': Wq, 'Wk': Wk, 'Wv': Wv, 'Wo': Wo}
    _L0_gnn_all = _L0_gnn_setup()
    _L0_gnn_in = {k: v for k, v in _L0_gnn_all.items() if k in ('Wq', 'Wk', 'Wv', 'Wo')}
    del _L0_gnn_all
    return {'x': x, 'adj': adj, 'L0_gnn_Wq': _L0_gnn_in['Wq'], 'L0_gnn_Wk': _L0_gnn_in['Wk'], 'L0_gnn_Wv': _L0_gnn_in['Wv'], 'L0_gnn_Wo': _L0_gnn_in['Wo']}

def reference(x, adj, L0_gnn_Wq, L0_gnn_Wk, L0_gnn_Wv, L0_gnn_Wo):
    import jax
    import jax.numpy as jnp

    def _L0_gnn_ref(x, adj, Wq, Wk, Wv, Wo):
        import jax, jax.numpy as jnp
        import numpy as np
        B, N, D = (8, 512, 256)
        NH = 8
        DK = D // NH
        b, n, d = x.shape
        sqrt_dk = jnp.asarray(np.sqrt(DK), dtype=x.dtype)

        def heads(t):
            return t.reshape(b, n, NH, DK).transpose(0, 2, 1, 3)
        q = heads(x @ Wq)
        k = heads(x @ Wk)
        v = heads(x @ Wv)
        scores = jnp.einsum('bhnd,bhmd->bhnm', q, k) / sqrt_dk
        mask = adj.astype(bool)[:, None]
        scores = jnp.where(mask, scores, -jnp.inf)
        attn = jax.nn.softmax(scores, axis=-1)
        out = jnp.einsum('bhnm,bhmd->bhnd', attn, v)
        out = out.transpose(0, 2, 1, 3).reshape(b, n, d)
        return jax.nn.relu(out) @ Wo
    x = _layernorm(x + _L0_gnn_ref(x, adj, L0_gnn_Wq, L0_gnn_Wk, L0_gnn_Wv, L0_gnn_Wo), axis=-1)
    return x

_drawn_inputs = setup_inputs


def setup_inputs(seed=0):
    import zlib

    import numpy as np

    out = dict(_drawn_inputs(seed))
    spreads = {}
    factors = {}
    for name, (base, spread) in spreads.items():
        noise = np.random.default_rng([zlib.crc32(name.encode()), seed]).standard_normal(out[name].shape)
        drawn = base * np.exp(spread * noise) if base else spread * noise
        out[name] = jnp.asarray(drawn.astype(out[name].dtype))
    for name, factor in factors.items():
        out[name] = (out[name] * factor).astype(out[name].dtype)
    return out
```

```python
from contextlib import ExitStack

import concourse.bass as bass
from concourse import mybir

F32 = mybir.dt.float32
F32R = mybir.dt.float32r
BF16 = mybir.dt.bfloat16
I32 = mybir.dt.int32
ALU = mybir.AluOpType
ACT = mybir.ActivationFunctionType

B, N, D, H = 16, 512, 256, 8
DK = D // H
P = 128
NT = N // P
KT = D // P
HG = P // DK
G = H // HG
TILES = H * NT
ROWS = 3 * DK
SCALE = 1.0 / float(DK) ** 0.5
MASKED = -1.0e30
EPS = 1e-5
PACKS = 6 * HG * 16
FIRST, LAST = -3, B
LOOP_FROM, LOOP_TO = 2, B - 4


class Batch:

    def __init__(self, off, j=None, low=0):
        self.off, self.j, self.low = off, j, low

    def plus(self, n):
        return Batch(self.off + n, self.j, self.low)

    @property
    def parity(self):
        return self.off % 2

    @property
    def exists(self):
        return self.j is not None or 0 <= self.off < B

    def count(self, per_batch, k):
        if self.j is None:
            return self.off * per_batch + k
        assert 2 * self.low * per_batch + self.off * per_batch + k > 0
        return self.j * (2 * per_batch) + (self.off * per_batch + k)

    def count_of_parity(self, per_batch, k):
        if self.j is None:
            return (self.off // 2) * per_batch + k
        assert (self.low + self.off // 2) * per_batch + k > 0
        return self.j * per_batch + ((self.off // 2) * per_batch + k)

    @property
    def index(self):
        return self.off if self.j is None else self.j * 2 + self.off


def wait(eng, sem, value):
    if not isinstance(value, int) or value > 0:
        eng.wait_ge(sem, value)


def wait_apart(eng, sem, value, passed):
    if not isinstance(value, int) or value > 0:
        eng.wait_ge(sem, value).then_inc(passed, 1)


def run_periods(eng, period):
    for b in range(FIRST, LOOP_FROM):
        period(Batch(b))
    with eng.Fori(LOOP_FROM // 2, LOOP_TO // 2) as j:
        for off in range(2):
            period(Batch(off, j, LOOP_FROM // 2))
    for b in range(LOOP_TO, LAST + 1):
        period(Batch(b))


SHORT = [
    (0, 1, "x_t", 0, 2), (0, 3, "x_t", 1, 2),
    (1, 1, "max_t", 1, 0), (1, 3, "qk", 0, 2),
    (2, 1, "qk", 1, 2),
    (3, 1, "qk", 2, 2), (3, 3, "qk", 3, 2),
    (4, 1, "out", 0, -1), (4, 3, "out", 1, -1),
    (5, 1, "max_t", 0, 1), (5, 3, "mask_t", 0, 1),
    (6, 1, "mask_t", 1, 1),
    (7, 1, "v", 0, 1), (7, 3, "v", 1, 1),
]


def graph_attention(nc, x, adj, wq, wk, wv, wo, out):
    with ExitStack() as ctx:
        def sb(name, shape, dt):
            return ctx.enter_context(nc.sbuf_tensor(name, shape, dt))

        def psum(name):
            return ctx.enter_context(nc.psum_tensor(name, [P, 512], F32))

        def sem(name):
            return ctx.enter_context(nc.semaphore(name))

        w_sb = {n: sb(f"w_{n}", [P, KT, D], F32) for n in "qkvo"}
        ident = sb("ident", [P, P], F32)
        ident_bf = sb("ident_bf", [P, P], BF16)
        ones = sb("ones", [P, DK], F32)
        minus_half = sb("minus_half", [P, NT], F32)
        x_in = sb("x_in", [P, NT, D], F32)
        adj_in = sb("adj_in", [P, NT // 2, N], I32)
        y = sb("y", [P, NT, D], F32)
        mask = [sb(f"mask{p}", [P, NT, N], BF16) for p in range(2)]
        mask_t = [sb(f"mask_t{p}", [P, NT, N], BF16) for p in range(2)]
        x_t = [sb(f"x_t{p}", [P, KT, N], F32) for p in range(2)]
        hi = [[sb(f"hi_{n}{g}", [P, N], F32R) for g in range(G)] for n in "qk"]
        lo = [[sb(f"lo_{n}{g}", [P, N], F32R) for g in range(G)] for n in "qk"]
        q_pack = [sb(f"q_pack{p}", [P, H, N], F32R) for p in range(2)]
        k_pack = [sb(f"k_pack{p}", [P, H, N], F32R) for p in range(2)]
        v_sb = [sb(f"v_sb{p}", [P, NT, D], F32) for p in range(2)]
        row_max = [sb(f"row_max{p}", [P, NT, H], F32) for p in range(2)]
        neg_max_hi = sb("neg_max_hi", [HG, N], F32R)
        neg_max_lo = sb("neg_max_lo", [HG, N], F32R)
        probs_t = sb("probs_t", [P, H - 1, NT, N], F32)
        probs_sum = sb("probs_sum", [P, HG, N], F32)
        inv_den = sb("inv_den", [P, N], F32)
        attn_t = [sb(f"attn_t{g}", [P, N], F32) for g in range(G)]
        stats = sb("stats", [P, NT, 6], F32)
        mean_var = sb("mean_var", [P, NT, 2], F32)
        var_eps = sb("var_eps", [P, NT], F32)
        rstd = sb("rstd", [P, NT], F32)

        ps_s = [psum(f"ps_s{i}") for i in range(2)]
        ps_st = [psum(f"ps_st{i}") for i in range(2)]
        ps_pv = psum("ps_pv")
        ps_den = psum("ps_den")
        ps_short = [psum(f"ps_short{i}") for i in range(2)]

        w_loaded = sem("w_loaded")
        x_loaded = sem("x_loaded")
        adj_loaded = sem("adj_loaded")
        residual_loaded = sem("residual_loaded")
        packs_laid = [[sem(f"packs_laid{p}{g}") for g in range(G)] for p in range(2)]
        max_laid = [[sem(f"max_laid{p}{g}") for g in range(G)] for p in range(2)]
        out_stored = sem("out_stored")
        x_t_ready = sem("x_t_ready")
        qk_ready = sem("qk_ready")
        max_t_ready = sem("max_t_ready")
        mask_t_ready = sem("mask_t_ready")
        v_ready = sem("v_ready")
        out_ready = sem("out_ready")
        scores_ready = sem("scores_ready")
        scores_t_ready = sem("scores_t_ready")
        den_ready = sem("den_ready")
        pv_ready = sem("pv_ready")
        x_t_copied = sem("x_t_copied")
        hi_copied = sem("hi_copied")
        max_hi_copied = sem("max_hi_copied")
        mask_t_copied = sem("mask_t_copied")
        v_copied = sem("v_copied")
        probs_ready = sem("probs_ready")
        consts_made = sem("consts_made")
        mask_made = sem("mask_made")
        lo_copied = sem("lo_copied")
        max_lo_copied = sem("max_lo_copied")
        max_done = sem("max_done")
        inv_den_made = sem("inv_den_made")
        attn_ready = sem("attn_ready")
        residual_added = sem("residual_added")
        stats_made = sem("stats_made")
        mean_var_made = sem("mean_var_made")
        var_eps_made = sem("var_eps_made")
        normed = sem("normed")
        dve_passed = sem("dve_passed")
        sp_passed = sem("sp_passed")
        zeroed = sem("zeroed")
        idents_made = sem("idents_made")
        partly_summed = sem("partly_summed")
        probs_summed = sem("probs_summed")
        rstd_made = sem("rstd_made")

        def buffer_of(h):
            return h if h < H - 1 else HG - 1

        x_v = x.rearrange("b (t p) d -> b p t d", p=P)
        adj_v = adj.rearrange("b (t p) m -> b p t m", p=P)
        out_v = out.rearrange("b (t p) d -> b p t d", p=P)

        SHORT_READ = {"x_t": (x_t_copied, 2), "qk": (lo_copied, 4), "max_t": (max_lo_copied, 2),
                      "mask_t": (mask_t_copied, 2), "v": (v_copied, 2), "out": (residual_added, 2)}

        def wait_short_bank(eng, b, i):
            while True:
                i -= 2
                if i < 0:
                    b, i = b.plus(-1), i + len(SHORT)
                if b.j is None and b.off < FIRST:
                    return
                _, _, job, part, rel = SHORT[i]
                if b.plus(rel).exists:
                    s, per = SHORT_READ[job]
                    wait(eng, s, b.plus(rel).count(per, part + 1))
                    return

        block = ctx.enter_context(nc.Block())

        @block.sync
        def _(sp):
            for n, w in zip("qkvo", (wq, wk, wv, wo)):
                sp.dma_start(w_sb[n][:, :, :], w.rearrange("(k p) n -> p k n", p=P)).then_inc(w_loaded, 16)

            def lay_out(b, prev, h):
                g, r = h // HG, (h % HG) * DK
                if h % HG == 0:
                    wait_apart(sp, lo_copied, b.count(4, 2 * g + 2), sp_passed)
                if prev.exists:
                    wait(sp, scores_t_ready, prev.count(TILES, NT * (h + 1)))
                for pack, srcs in ((q_pack, (hi[0], lo[0], hi[0])), (k_pack, (hi[1], hi[1], lo[1]))):
                    for c, src in enumerate(srcs):
                        sp.dma_start(pack[b.parity][c * DK:(c + 1) * DK, h, :].bitcast(F32),
                                     src[g][r:r + DK, :].bitcast(F32)).then_inc(packs_laid[b.parity][g], 16)

            def load_adj(b, half):
                wait_apart(sp, mask_made, b.count(2, half), sp_passed)
                sp.dma_start(adj_in[:, :, :], adj_v[b.index, :, 2 * half:2 * half + 2, :]).then_inc(adj_loaded, 16)

            def period(b):
                nx, pk, last = b.plus(3), b.plus(2), b.plus(-1)
                if nx.exists:
                    wait_apart(sp, x_t_ready, nx.count(2, 0), sp_passed)
                    sp.dma_start(x_in[:, :, :], x_v[nx.index]).then_inc(x_loaded, 16)
                if last.exists:
                    wait_apart(sp, out_stored, last.count(16, 0), sp_passed)
                    sp.dma_start(y[:, :, :], x_v[last.index]).then_inc(residual_loaded, 16)
                if pk.exists:
                    lay_out(pk, b, 0)
                    load_adj(pk, 1)
                    for h in range(1, HG):
                        lay_out(pk, b, h)
                if nx.exists:
                    load_adj(nx, 0)
                if pk.exists:
                    for h in range(HG, H - 1):
                        lay_out(pk, b, h)
                if last.exists:
                    wait_apart(sp, normed, last.count(1, 1), sp_passed)
                    sp.dma_start(out_v[last.index], y[:, :, :]).then_inc(out_stored, 16)
                if pk.exists:
                    lay_out(pk, b, H - 1)

            run_periods(sp, period)
            sp.wait_ge(out_stored, 16 * B)

        @block.tensor
        def _(pe):
            pe.wait_ge(idents_made, 2)
            pe.wait_ge(consts_made, 1)
            pe.wait_ge(w_loaded, 64)

            def scores(b, h, t):
                if h % HG == 0 and t == 0:
                    wait(pe, packs_laid[b.parity][h // HG], b.count_of_parity(PACKS, PACKS))
                wait(pe, max_done, b.count(TILES, NT * h + t - 1))
                pe.matmul(ps_s[t % 2][:, :], q_pack[b.parity][0:ROWS, h, t * P:(t + 1) * P],
                          k_pack[b.parity][0:ROWS, h, :], start=True, stop=True).then_inc(scores_ready, 1)

            def scores_transposed(b, h, t):
                if h % HG == 0 and t == 0:
                    wait(pe, max_laid[b.parity][h // HG], b.count_of_parity(32, 32))
                if h == 0 and t == 0:
                    wait(pe, mask_t_copied, b.count(2, 2))
                wait(pe, probs_ready, b.count(TILES, NT * h + t - 1))
                pe.matmul(ps_st[t % 2][:, :], k_pack[b.parity][0:ROWS + 2, h, t * P:(t + 1) * P],
                          q_pack[b.parity][0:ROWS + 2, h, :], start=True, stop=False)
                pe.matmul(ps_st[t % 2][:, :], ident_bf[:, :], mask_t[b.parity][:, t, :],
                          start=False, stop=True).then_inc(scores_t_ready, 1)

            def probs_times_v(b, g, t):
                if t == 0:
                    wait(pe, probs_ready, b.count(TILES, NT * HG * (g + 1)))
                    wait(pe, v_copied, b.count(2, 2))
                for i in range(HG):
                    h = g * HG + i
                    mm = pe.matmul(ps_pv[i * DK:(i + 1) * DK, :], v_sb[b.parity][:, t, h * DK:(h + 1) * DK],
                                   probs_t[:, buffer_of(h), t, :], start=(t == 0), stop=(t == NT - 1))
                if t == NT - 1:
                    mm.then_inc(pv_ready, 1)

            def denominators(b, g):
                wait(pe, probs_summed, b.count(H, HG * (g + 1)))
                wait(pe, attn_ready, b.count(2, g))
                for i in range(HG):
                    mm = pe.matmul(ps_den[i * DK:(i + 1) * DK, :], ones[:, :], probs_sum[:, i, :],
                                   start=True, stop=True)
                mm.then_inc(den_ready, 1)

            def x_transposed(b, k, bank):
                pe.wait_ge(x_loaded, b.count(16, 16))
                for t in range(NT):
                    mm = pe.transpose(bank[:, t * P:(t + 1) * P], x_in[:, t, k * P:(k + 1) * P], ident[:, :])
                mm.then_inc(x_t_ready, 1)

            def project_qk(b, u, bank):
                wait(pe, x_t_copied, b.count(2, 2))
                g = u // 2
                for k in range(KT):
                    mm = pe.matmul(bank[:, :], w_sb["qk"[u % 2]][:, k, g * P:(g + 1) * P], x_t[b.parity][:, k, :],
                                   start=(k == 0), stop=(k == KT - 1))
                mm.then_inc(qk_ready, 1)

            def project_v(b, u, bank):
                for t in (2 * u, 2 * u + 1):
                    for k in range(KT):
                        mm = pe.matmul(bank[:, (t % 2) * D:(t % 2 + 1) * D], x_t[b.parity][:, k, t * P:(t + 1) * P],
                                       w_sb["v"][:, k, :], start=(k == 0), stop=(k == KT - 1))
                mm.then_inc(v_ready, 1)

            def max_transposed(b, g, bank):
                wait(pe, max_done, b.count(TILES, NT * HG * (g + 1)))
                for t in range(NT):
                    mm = pe.transpose(bank[0:HG, t * P:(t + 1) * P], row_max[b.parity][:, t, g * HG:(g + 1) * HG],
                                      ident[:, :])
                mm.then_inc(max_t_ready, 1)

            def mask_transposed(b, u, bank):
                wait(pe, mask_made, b.count(2, 2))
                half = bank[:, :].bitcast(BF16)
                for mt in (2 * u, 2 * u + 1):
                    for t in range(NT):
                        at = (mt % 2) * N + t * P
                        mm = pe.transpose(half[:, at:at + P], mask[b.parity][:, t, mt * P:(mt + 1) * P], ident_bf[:, :])
                mm.then_inc(mask_t_ready, 1)

            def project_out(b, u, bank):
                wait(pe, attn_ready, b.count(2, 2))
                for t in (2 * u, 2 * u + 1):
                    for g in range(G):
                        mm = pe.matmul(bank[:, (t % 2) * D:(t % 2 + 1) * D], attn_t[g][:, t * P:(t + 1) * P],
                                       w_sb["o"][:, g, :], start=(g == 0), stop=(g == G - 1))
                mm.then_inc(out_ready, 1)

            jobs = {"x_t": x_transposed, "qk": project_qk, "v": project_v, "max_t": max_transposed,
                    "mask_t": mask_transposed, "out": project_out}

            def period(b):
                for h in range(H):
                    for t in range(NT):
                        if b.exists:
                            scores_transposed(b, h, t)
                        if b.plus(1).exists:
                            scores(b.plus(1), h, t)
                        for i, (slot, after, job, part, rel) in enumerate(SHORT):
                            if (slot, after) == (h, t) and b.plus(rel).exists:
                                wait_short_bank(pe, b, i)
                                jobs[job](b.plus(rel), part, ps_short[i % 2])
                        if t == 2:
                            for slot, pb, g in ((1, b.plus(-1), 1), (5, b, 0)):
                                if pb.exists and h == slot:
                                    denominators(pb, g)
                                    probs_times_v(pb, g, 0)
                                    probs_times_v(pb, g, 1)
                                if pb.exists and h == slot + 1:
                                    probs_times_v(pb, g, 2)
                                    probs_times_v(pb, g, 3)

            run_periods(pe, period)

        @block.scalar
        def _(act):
            def probs(b, h, t):
                if t == 0 and h in (0, HG - 1, H - 1):
                    wait(act, pv_ready, b.count(2, {0: -1, HG - 1: 0, H - 1: 1}[h]))
                act.wait_ge(scores_t_ready, b.count(TILES, NT * h + t + 1))
                act.activation(probs_t[:, buffer_of(h), t, :], ps_st[t % 2][:, :], ACT.Exp,
                               scale=SCALE).then_inc(probs_ready, 1)

            def copy_x_t(b, k, bank):
                wait(act, v_ready, b.count(2, -2))
                act.wait_ge(x_t_ready, b.count(2, k + 1))
                act.copy(x_t[b.parity][:, k, :], bank[:, :]).then_inc(x_t_copied, 1)

            def copy_hi(b, u, bank):
                g, prev = u // 2, b.plus(-1)
                wait(act, packs_laid[prev.parity][g], prev.count_of_parity(PACKS, PACKS))
                act.wait_ge(qk_ready, b.count(4, u + 1))
                act.copy(hi[u % 2][g][:, :], bank[:, :]).then_inc(hi_copied, 1)

            def copy_v(b, u, bank):
                wait(act, pv_ready, b.count(2, -2))
                act.wait_ge(v_ready, b.count(2, u + 1))
                act.copy(v_sb[b.parity][:, 2 * u:2 * u + 2, :],
                         bank[:, :].rearrange("p (t d) -> p t d", t=2)).then_inc(v_copied, 1)

            def copy_max_hi(b, g, bank):
                if g == 1:
                    act.wait_ge(max_laid[b.parity][0], b.count_of_parity(32, 32))
                elif b.plus(-1).exists:
                    act.wait_ge(max_laid[b.plus(-1).parity][1], b.plus(-1).count_of_parity(32, 32))
                act.wait_ge(max_t_ready, b.count(2, g + 1))
                act.mul(neg_max_hi[:, :], bank[0:HG, :], -1.0).then_inc(max_hi_copied, 1)

            def copy_mask_t(b, u, bank):
                wait(act, scores_t_ready, b.count(TILES, -TILES))
                act.wait_ge(mask_t_ready, b.count(2, u + 1))
                act.copy(mask_t[b.parity][:, 2 * u:2 * u + 2, :],
                         bank[:, :].bitcast(BF16).rearrange("p (t n) -> p t n", t=2)).then_inc(mask_t_copied, 1)

            def lay_out_max(b, g):
                act.wait_ge(max_lo_copied, b.count(2, g + 1))
                for r, src in enumerate((neg_max_hi, neg_max_lo)):
                    act.dma_start(q_pack[b.parity][ROWS + r:ROWS + r + 1, g * HG:(g + 1) * HG, :].bitcast(F32),
                                  src[:, :].bitcast(F32)).then_inc(max_laid[b.parity][g], 16)

            jobs = {"x_t": copy_x_t, "qk": copy_hi, "v": copy_v, "max_t": copy_max_hi, "mask_t": copy_mask_t}

            def period(b):
                for h in range(H):
                    for t in range(NT):
                        if b.exists:
                            probs(b, h, t)
                        if (h, t) == (1, 3) and b.exists:
                            lay_out_max(b, 1)
                        if (h, t) == (5, 3) and b.plus(1).exists:
                            lay_out_max(b.plus(1), 0)
                        for i, (slot, after, job, part, rel) in enumerate(SHORT):
                            if (slot, after) == (h, t) and b.plus(rel).exists and job in jobs:
                                jobs[job](b.plus(rel), part, ps_short[i % 2])

            run_periods(act, period)

        @block.vector
        def _(dve):
            for p in range(2):
                dve.memset(k_pack[p][ROWS:P, :, :].bitcast(F32), 1.0)
            dve.memset(minus_half[:, :], -0.5)
            dve.memset(ones[:, :], 1.0).then_inc(consts_made, 1)

            def maximum(b, h, t):
                if h == 0 and t == 0:
                    wait(dve, max_t_ready, b.count(2, -2))
                    dve.wait_ge(mask_made, b.count(2, 2))
                wait_apart(dve, scores_ready, b.count(TILES, NT * h + t + 1), dve_passed)
                dve.tensor_tensor_reduce(ps_s[t % 2][:, :], ps_s[t % 2][:, :], mask[b.parity][:, t, :], 1.0, -3.0e38,
                                         ALU.add, ALU.max, row_max[b.parity][:, t, h:h + 1]).then_inc(max_done, 1)

            def make_mask(b, half):
                if half == 0:
                    wait(dve, mask_t_ready, b.count(2, -2))
                dve.wait_ge(adj_loaded, b.count(32, 16 * half + 16))
                dve.tensor_scalar(mask[b.parity][:, 2 * half:2 * half + 2, :], adj_in[:, :, :], 0, MASKED,
                                  ALU.is_equal, ALU.mult).then_inc(mask_made, 1)

            def copy_lo(b, u, bank):
                dve.wait_ge(hi_copied, b.count(4, u + 1))
                dve.tensor_tensor(lo[u % 2][u // 2][:, :], bank[:, :], hi[u % 2][u // 2][:, :].bitcast(F32),
                                  ALU.subtract).then_inc(lo_copied, 1)

            def copy_max_lo(b, g, bank):
                dve.wait_ge(max_hi_copied, b.count(2, g + 1))
                dve.scalar_tensor_tensor(out=neg_max_lo[:, :], in0=bank[0:HG, :], scalar=-1.0,
                                         in1=neg_max_hi[:, :].bitcast(F32), op0=ALU.mult,
                                         op1=ALU.subtract).then_inc(max_lo_copied, 1)

            def normalise(b, g):
                dve.wait_ge(pv_ready, b.count(2, g + 1))
                dve.reciprocal(inv_den[:, :], ps_den[:, :]).then_inc(inv_den_made, 1)
                wait(dve, out_ready, b.count(2, 0))
                dve.wait_ge(inv_den_made, b.count(2, g + 1))
                dve.scalar_tensor_tensor(out=attn_t[g][:, :], in0=ps_pv[:, :], scalar=0.0, in1=inv_den[:, :],
                                         op0=ALU.max, op1=ALU.mult).then_inc(attn_ready, 1)

            def add_residual(b, u, bank):
                dve.wait_ge(residual_loaded, b.count(16, 16))
                dve.wait_ge(out_ready, b.count(2, u + 1))
                rows = y[:, 2 * u:2 * u + 2, :].rearrange("p t d -> p (t d)")
                dve.tensor_tensor(rows, bank[:, :], rows, ALU.add).then_inc(residual_added, 1)

            def statistics(b, t):
                dve.wait_ge(residual_added, b.count(2, t // 2 + 1))
                dve.bn_stats(stats[:, t, :], y[:, t, :]).then_inc(stats_made, 1)

            def mean_and_variance(b):
                wait_apart(dve, stats_made, b.count(NT, NT), dve_passed)
                for t in range(NT):
                    ins = dve.bn_aggr(mean_var[:, t, :], stats[:, t, :])
                ins.then_inc(mean_var_made, 1)
                dve.wait_ge(mean_var_made, b.count(1, 1))
                dve.tensor_scalar(var_eps[:, :], mean_var[:, :, 1], EPS, None, ALU.add).then_inc(var_eps_made, 1)

            def normalise_rows(b):
                dve.wait_ge(rstd_made, b.count(1, 1))
                for t in range(NT):
                    ins = dve.tensor_scalar(y[:, t, :], y[:, t, :], mean_var[:, t, 0:1],
                                            rstd[:, t:t + 1], ALU.subtract, ALU.mult)
                ins.then_inc(normed, 1)

            jobs = {"qk": copy_lo, "max_t": copy_max_lo, "out": add_residual}

            def period(b):
                last = b.plus(-1)
                for h in range(H):
                    for t in range(NT):
                        if b.plus(1).exists:
                            maximum(b.plus(1), h, t)
                        if h in (1, 3) and t == 2 and b.plus(2).exists:
                            make_mask(b.plus(2), h // 2)
                        if (h, t) == (3, 0) and last.exists:
                            normalise(last, 1)
                        if (h, t) == (7, 0) and b.exists:
                            normalise(b, 0)
                        if h == 5 and last.exists:
                            statistics(last, t)
                        if (h, t) == (6, 0) and last.exists:
                            mean_and_variance(last)
                        if (h, t) == (7, 2) and last.exists:
                            normalise_rows(last)
                        for i, (slot, after, job, part, rel) in enumerate(SHORT):
                            if (slot, after) == (h, t) and b.plus(rel).exists and job in jobs:
                                jobs[job](b.plus(rel), part, ps_short[i % 2])

            run_periods(dve, period)

        @block.gpsimd
        def _(pool):
            for n, idt in enumerate((ident, ident_bf)):
                pool.memset(idt[:, :], 0.0).then_inc(zeroed, 1)
                pool.wait_ge(zeroed, n + 1)
                pool.affine_select(out=idt[:, :], in_=idt[:, :], compare_op=ALU.not_equal, fill=1.0, base=0,
                                   pattern=[[-1, P]], channel_multiplier=1).then_inc(idents_made, 1)
            pool.wait_ge(consts_made, 1)

            def sum_probs(b, h):
                g, i = h // HG, h % HG
                if i == 0:
                    wait(pool, den_ready, b.count(2, g))
                pool.wait_ge(probs_ready, b.count(TILES, NT * (h + 1)))
                total, part = probs_sum[:, i, :], probs_t[:, buffer_of(h), :, :]
                pool.tensor_tensor(total, part[:, 0, :], part[:, 1, :], ALU.add).then_inc(partly_summed, 1)
                pool.wait_ge(partly_summed, b.count(2 * H, 2 * h + 1))
                pool.tensor_tensor(total, total, part[:, 2, :], ALU.add).then_inc(partly_summed, 1)
                pool.wait_ge(partly_summed, b.count(2 * H, 2 * h + 2))
                pool.tensor_tensor(total, total, part[:, 3, :], ALU.add).then_inc(probs_summed, 1)

            def period(b):
                last = b.plus(-1)
                for h in range(H):
                    if b.exists:
                        sum_probs(b, h)
                    if h == 5 and last.exists:
                        pool.wait_ge(var_eps_made, last.count(1, 1))
                        pool.tensor_tensor(rstd[:, :], var_eps[:, :], minus_half[:, :], ALU.pow).then_inc(rstd_made, 1)

            run_periods(pool, period)


def kernel(x, adj, L0_gnn_Wq, L0_gnn_Wk, L0_gnn_Wv, L0_gnn_Wo):
    import numpy as np
    import concourse.bacc as bacc
    from concourse.bass_utils import run_bass_kernel_spmd

    nc = bacc.Bacc("TRN2", target_bir_lowering=False, num_devices=1)
    arrays = {"in_x": x, "in_adj": adj, "in_wq": L0_gnn_Wq, "in_wk": L0_gnn_Wk, "in_wv": L0_gnn_Wv, "in_wo": L0_gnn_Wo}
    arrays = {name: np.ascontiguousarray(a) for name, a in arrays.items()}
    ins = [nc.dram_tensor(name, a.shape, mybir.dt.from_np(a.dtype), kind="ExternalInput").ap()
           for name, a in arrays.items()]
    out = nc.dram_tensor("out", (B, N, D), F32, kind="ExternalOutput").ap()
    graph_attention(nc, *ins, out)
    result = run_bass_kernel_spmd(nc, [arrays], core_ids=[0])
    return result.results[0]["out"]
```

```python
from contextlib import ExitStack

import concourse.bass as bass
from concourse import mybir

F32 = mybir.dt.float32
F32R = mybir.dt.float32r
BF16 = mybir.dt.bfloat16
I32 = mybir.dt.int32
ALU = mybir.AluOpType
ACT = mybir.ActivationFunctionType

B, N, D, H = 16, 512, 256, 8
DK = D // H
P = 128
NT = N // P
KT = D // P
HG = P // DK
G = H // HG
TILES = H * NT
ROWS = 3 * DK
SCALE = 1.0 / float(DK) ** 0.5
MASKED = -1.0e30
EPS = 1e-5
PACKS = 6 * 16
SEEDED = (0, 1, 2, 3)
AHEAD = 2
ST_BANKS = 3
FIRST, LAST = -3, B
LOOP_FROM, LOOP_TO = 2, B - 4


class Batch:

    def __init__(self, off, j=None, low=0):
        self.off, self.j, self.low = off, j, low

    def plus(self, n):
        return Batch(self.off + n, self.j, self.low)

    @property
    def parity(self):
        return self.off % 2

    @property
    def exists(self):
        return self.j is not None or 0 <= self.off < B

    def count(self, per_batch, k):
        if self.j is None:
            return self.off * per_batch + k
        assert 2 * self.low * per_batch + self.off * per_batch + k > 0
        return self.j * (2 * per_batch) + (self.off * per_batch + k)

    def count_of_parity(self, per_batch, k):
        if self.j is None:
            return (self.off // 2) * per_batch + k
        assert (self.low + self.off // 2) * per_batch + k > 0
        return self.j * per_batch + ((self.off // 2) * per_batch + k)

    @property
    def index(self):
        return self.off if self.j is None else self.j * 2 + self.off


def wait(eng, sem, value):
    if not isinstance(value, int) or value > 0:
        eng.wait_ge(sem, value)


def wait_apart(eng, sem, value, passed):
    if not isinstance(value, int) or value > 0:
        eng.wait_ge(sem, value).then_inc(passed, 1)


def run_periods(eng, period):
    for b in range(FIRST, LOOP_FROM):
        period(Batch(b))
    with eng.Fori(LOOP_FROM // 2, LOOP_TO // 2) as j:
        for off in range(2):
            period(Batch(off, j, LOOP_FROM // 2))
    for b in range(LOOP_TO, LAST + 1):
        period(Batch(b))


EXTRA = [
    ("x_t", 0, 0, 2), ("x_t", 1, 0, 2), ("mask_t", 0, 0, 1), ("max_t", 1, 0, 0),
    ("pv", 1, 0, -1), ("den", 1, 0, -1), ("pv", 1, 1, -1), ("pv", 1, 2, -1),
    ("pv", 1, 3, -1), ("qk", 0, 0, 2), ("qk", 0, 1, 2), ("mask_t", 1, 0, 1),
    ("qk", 1, 0, 2), ("qk", 1, 1, 2), ("v", 0, 0, 1), ("v", 0, 1, 1),
    ("out", 0, 0, -1), ("out", 0, 1, -1), ("out", 1, 0, -1), ("out", 1, 1, -1),
    ("pv", 0, 0, 0), ("den", 0, 0, 0), ("pv", 0, 1, 0), ("pv", 0, 2, 0),
    ("pv", 0, 3, 0), ("max_t", 0, 0, 1), ("qk", 2, 0, 2), ("qk", 2, 1, 2),
    ("qk", 3, 0, 2), ("qk", 3, 1, 2), ("v", 1, 0, 1), ("v", 1, 1, 1),
]
SHORT = [(job, part, rel) for job, part, piece, rel in EXTRA if job != "pv" and piece == 0]
SCALAR_EXTRA = {0: ("x_t", 0, 2), 1: ("x_t", 1, 2), 2: ("mask_t", 0, 1), 3: ("max_t", 1, 0),
                10: ("qk", 0, 2), 11: ("mask_t", 1, 1), 13: ("qk", 1, 2), 15: ("v", 0, 1), 25: ("max_t", 0, 1),
                27: ("qk", 2, 2), 29: ("qk", 3, 2), 31: ("v", 1, 1)}
VECTOR_EXTRA = [(2, "mask", 0, 2), (5, "inv", (1, 0), -1), (6, "inv", (1, 1), -1), (6, "inv", (1, 2), -1),
                (7, "inv", (1, 3), -1), (10, "attn", 1, -1), (11, "qk", 0, 2), (14, "qk", 1, 2), (15, "mask", 1, 2),
                (18, "out", 0, -1), (19, "stats", 0, -1), (20, "out", 1, -1), (21, "inv", (0, 0), 0),
                (22, "inv", (0, 1), 0), (22, "inv", (0, 2), 0), (23, "inv", (0, 3), 0), (24, "stats", 1, -1),
                (24, "mean", 0, -1), (26, "attn", 0, 0), (28, "qk", 2, 2), (30, "qk", 3, 2), (31, "rows", 0, -1)]


def graph_attention(nc, x, adj, wq, wk, wv, wo, out):
    with ExitStack() as ctx:
        def sb(name, shape, dt):
            return ctx.enter_context(nc.sbuf_tensor(name, shape, dt))

        def psum(name):
            return ctx.enter_context(nc.psum_tensor(name, [P, 512], F32))

        def sem(name):
            return ctx.enter_context(nc.semaphore(name))

        w_sb = {n: sb(f"w_{n}", [P, KT, D], F32) for n in "qkvo"}
        ident = sb("ident", [P, P], F32)
        ident_bf = sb("ident_bf", [P, P], BF16)
        ones = sb("ones", [P, DK], F32)
        minus_half = sb("minus_half", [P, NT], F32)
        x_in = sb("x_in", [P, NT, D], F32)
        adj_in = sb("adj_in", [P, NT // 2, N], I32)
        y = sb("y", [P, NT, D], F32)
        mask = [sb(f"mask{p}", [P, NT, N], BF16) for p in range(2)]
        mask_t = [sb(f"mask_t{p}", [P, NT, N], BF16) for p in range(2)]
        x_t = [sb(f"x_t{p}", [P, KT, N], F32) for p in range(2)]
        hi = [[sb(f"hi_{n}{g}", [P, N], F32R) for g in range(G)] for n in "qk"]
        lo = [[sb(f"lo_{n}{g}", [P, N], F32R) for g in range(G)] for n in "qk"]
        q_pack = [sb(f"q_pack{p}", [P, H, N], F32R) for p in range(2)]
        k_pack = [sb(f"k_pack{p}", [P, H, N], F32R) for p in range(2)]
        v_sb = [sb(f"v_sb{p}", [P, NT, D], F32) for p in range(2)]
        row_max = [sb(f"row_max{p}", [P, NT, H], F32) for p in range(2)]
        neg_max = sb("neg_max", [HG, N], F32R)
        probs_t = sb("probs_t", [P, H - 1, NT, N], F32)
        probs_sum = sb("probs_sum", [P, HG, N], F32)
        inv_den = sb("inv_den", [P, N], F32)
        attn_t = [sb(f"attn_t{g}", [P, N], F32) for g in range(G)]
        stats = sb("stats", [P, NT, 6], F32)
        mean_var = sb("mean_var", [P, NT, 2], F32)
        var_eps = sb("var_eps", [P, NT], F32)
        rstd = sb("rstd", [P, NT], F32)

        ps_s = [psum(f"ps_s{i}") for i in range(2)]
        ps_st = [psum(f"ps_st{i}") for i in range(ST_BANKS)]
        ps_pv = psum("ps_pv")
        ps_short = [psum(f"ps_short{i}") for i in range(2)]

        w_loaded = sem("w_loaded")
        x_loaded = sem("x_loaded")
        adj_loaded = sem("adj_loaded")
        residual_loaded = sem("residual_loaded")
        packs_laid = [[sem(f"packs_laid{p}{g}") for g in range(G)] for p in range(2)]
        max_laid = [[sem(f"max_laid{p}{g}") for g in range(G)] for p in range(2)]
        out_stored = sem("out_stored")
        bits_set = sem("bits_set")
        x_t_ready = sem("x_t_ready")
        qk_ready = sem("qk_ready")
        max_t_ready = sem("max_t_ready")
        mask_t_ready = sem("mask_t_ready")
        v_ready = sem("v_ready")
        out_ready = sem("out_ready")
        scores_ready = sem("scores_ready")
        scores_t_ready = sem("scores_t_ready")
        den_ready = sem("den_ready")
        pv_ready = sem("pv_ready")
        mask_seeded = sem("mask_seeded")
        x_t_copied = sem("x_t_copied")
        hi_copied = sem("hi_copied")
        max_copied = sem("max_copied")
        mask_t_copied = sem("mask_t_copied")
        v_copied = sem("v_copied")
        probs_ready = sem("probs_ready")
        consts_made = sem("consts_made")
        mask_made = sem("mask_made")
        lo_copied = sem("lo_copied")
        max_done = sem("max_done")
        inv_den_made = sem("inv_den_made")
        attn_ready = sem("attn_ready")
        residual_added = sem("residual_added")
        stats_made = sem("stats_made")
        mean_var_made = sem("mean_var_made")
        var_eps_made = sem("var_eps_made")
        normed = sem("normed")
        dve_passed = sem("dve_passed")
        sp_passed = sem("sp_passed")
        zeroed = sem("zeroed")
        idents_made = sem("idents_made")
        partly_summed = sem("partly_summed")
        probs_summed = sem("probs_summed")
        rstd_made = sem("rstd_made")

        def buffer_of(h):
            return h if h < H - 1 else HG - 1

        def bank_before(n):
            return n - ST_BANKS if n >= ST_BANKS else (TILES - 1 - (TILES - 1 - n) % ST_BANKS) - TILES

        x_v = x.rearrange("b (t p) d -> b p t d", p=P)
        adj_v = adj.rearrange("b (t p) m -> b p t m", p=P)
        out_v = out.rearrange("b (t p) d -> b p t d", p=P)

        SHORT_READ = {"x_t": (x_t_copied, 2), "qk": (lo_copied, 4), "max_t": (max_copied, 2),
                      "mask_t": (mask_t_copied, 2), "v": (v_copied, 2), "out": (residual_added, 2),
                      "den": (inv_den_made, 2 * NT)}

        def bank_of(job, part):
            return ps_short[[(j, p) for j, p, _ in SHORT].index((job, part)) % 2]

        def wait_short_bank(eng, b, i):
            while True:
                i -= 2
                if i < 0:
                    b, i = b.plus(-1), i + len(SHORT)
                if b.j is None and b.off < FIRST:
                    return
                job, part, rel = SHORT[i]
                if b.plus(rel).exists:
                    s, per = SHORT_READ[job]
                    each = NT if job == "den" else 1
                    wait(eng, s, b.plus(rel).count(per, each * (part + 1)))
                    return

        block = ctx.enter_context(nc.Block())

        @block.sync
        def _(sp):
            for n, w in zip("qkvo", (wq, wk, wv, wo)):
                sp.dma_start(w_sb[n][:, :, :], w.rearrange("(k p) n -> p k n", p=P)).then_inc(w_loaded, 16)

            def lay_out(b, prev, g):
                wait_apart(sp, lo_copied, b.count(4, 2 * g + 2), sp_passed)
                if prev.exists:
                    wait(sp, scores_t_ready, prev.count(TILES, NT * HG * (g + 1)))
                for pack, srcs in ((q_pack, (hi[0], lo[0], hi[0])), (k_pack, (hi[1], hi[1], lo[1]))):
                    for c, src in enumerate(srcs):
                        sp.dma_start(pack[b.parity][c * DK:(c + 1) * DK, g * HG:(g + 1) * HG, :].bitcast(F32),
                                     src[g][:, :].bitcast(F32)).then_inc(packs_laid[b.parity][g], 16)

            def lay_out_max(b, g):
                wait(sp, max_copied, b.count(2, g + 1))
                sp.dma_start(q_pack[b.parity][ROWS:ROWS + 1, g * HG:(g + 1) * HG, :].bitcast(F32),
                             neg_max[:, :].bitcast(F32)).then_inc(max_laid[b.parity][g], 16)

            def load_adj(b, half):
                wait_apart(sp, mask_made, b.count(2, half), sp_passed)
                sp.dma_start(adj_in[:, :, :], adj_v[b.index, :, 2 * half:2 * half + 2, :]).then_inc(adj_loaded, 16)

            def period(b):
                nx, pk, last = b.plus(3), b.plus(2), b.plus(-1)
                if nx.exists:
                    wait_apart(sp, x_t_ready, nx.count(2, 0), sp_passed)
                    sp.dma_start(x_in[:, :, :], x_v[nx.index]).then_inc(x_loaded, 16)
                if b.exists:
                    lay_out_max(b, 1)
                if last.exists:
                    wait_apart(sp, out_stored, last.count(16, 0), sp_passed)
                    sp.dma_start(y[:, :, :], x_v[last.index]).then_inc(residual_loaded, 16)
                if pk.exists:
                    load_adj(pk, 1)
                    lay_out(pk, b, 0)
                if nx.exists:
                    load_adj(nx, 0)
                if b.plus(1).exists:
                    lay_out_max(b.plus(1), 0)
                if last.exists:
                    wait_apart(sp, normed, last.count(1, 1), sp_passed)
                    sp.dma_start(out_v[last.index], y[:, :, :]).then_inc(out_stored, 16)
                if pk.exists:
                    lay_out(pk, b, 1)

            run_periods(sp, period)
            sp.wait_ge(out_stored, 16 * B)

        @block.tensor
        def _(pe):
            pe.wait_ge(idents_made, 2)
            pe.wait_ge(consts_made, 1)
            pe.wait_ge(w_loaded, 64)
            for bank in ps_st:
                for t in range(NT):
                    mm = pe.matmul(bank[:, t * P:(t + 1) * P], ident_bf[:, :], ident_bf[:, :], start=(t == 0),
                                   stop=(t == NT - 1), skip_group_check=True)
            mm.then_inc(bits_set, 1)

            def scores(b, h, t):
                if h % HG == 0 and t == 0:
                    wait(pe, packs_laid[b.parity][h // HG], b.count_of_parity(PACKS, PACKS))
                wait(pe, max_done, b.count(TILES, NT * h + t - 1))
                pe.matmul(ps_s[t % 2][:, :], q_pack[b.parity][0:ROWS, h, t * P:(t + 1) * P],
                          k_pack[b.parity][0:ROWS, h, :], start=True, stop=True).then_inc(scores_ready, 1)

            def scores_transposed(b, h, t):
                if h % HG == 0 and t == 0:
                    wait(pe, max_laid[b.parity][h // HG], b.count_of_parity(16, 16))
                bank, seeded = ps_st[(NT * h + t) % ST_BANKS], t in SEEDED
                if seeded:
                    pe.wait_ge(mask_seeded, b.count(len(SEEDED) * H, len(SEEDED) * h + SEEDED.index(t) + 1))
                else:
                    if h == 0:
                        pe.wait_ge(mask_t_copied, b.count(2, 2))
                    wait(pe, probs_ready, b.count(TILES, bank_before(NT * h + t) + 1))
                mm = pe.matmul(bank[:, :], k_pack[b.parity][0:ROWS + 1, h, t * P:(t + 1) * P],
                               q_pack[b.parity][0:ROWS + 1, h, :], start=not seeded, stop=seeded, skip_group_check=True)
                if not seeded:
                    mm = pe.matmul(bank[:, :], ident_bf[:, :], mask_t[b.parity][:, t, :], start=False, stop=True,
                                   skip_group_check=True)
                mm.then_inc(scores_t_ready, 1)

            def probs_times_v(b, g, t):
                if t == 0:
                    wait(pe, probs_ready, b.count(TILES, NT * HG * (g + 1)))
                    wait(pe, v_copied, b.count(2, 2))
                    wait(pe, attn_ready, b.count(2, g))
                for i in range(HG):
                    h = g * HG + i
                    mm = pe.matmul(ps_pv[i * DK:(i + 1) * DK, :], v_sb[b.parity][:, t, h * DK:(h + 1) * DK],
                                   probs_t[:, buffer_of(h), t, :], start=(t == 0), stop=(t == NT - 1))
                if t == NT - 1:
                    mm.then_inc(pv_ready, 1)

            def denominators(b, g, _, bank):
                wait(pe, probs_summed, b.count(H, HG * (g + 1)))
                for i in range(HG):
                    mm = pe.matmul(bank[i * DK:(i + 1) * DK, :], ones[:, :], probs_sum[:, i, :],
                                   start=True, stop=True)
                mm.then_inc(den_ready, 1)

            def x_transposed(b, k, _, bank):
                pe.wait_ge(x_loaded, b.count(16, 16))
                for t in range(NT):
                    mm = pe.transpose(bank[:, t * P:(t + 1) * P], x_in[:, t, k * P:(k + 1) * P], ident[:, :])
                mm.then_inc(x_t_ready, 1)

            def project_qk(b, u, k, bank):
                wait(pe, x_t_copied, b.count(2, 2))
                g = u // 2
                mm = pe.matmul(bank[:, :], w_sb["qk"[u % 2]][:, k, g * P:(g + 1) * P], x_t[b.parity][:, k, :],
                               start=(k == 0), stop=(k == KT - 1))
                if k == KT - 1:
                    mm.then_inc(qk_ready, 1)

            def project_v(b, u, i, bank):
                t = 2 * u + i
                for k in range(KT):
                    mm = pe.matmul(bank[:, i * D:(i + 1) * D], x_t[b.parity][:, k, t * P:(t + 1) * P],
                                   w_sb["v"][:, k, :], start=(k == 0), stop=(k == KT - 1))
                if i == 1:
                    mm.then_inc(v_ready, 1)

            def max_transposed(b, g, _, bank):
                wait(pe, max_done, b.count(TILES, NT * HG * (g + 1)))
                for t in range(NT):
                    mm = pe.transpose(bank[0:HG, t * P:(t + 1) * P], row_max[b.parity][:, t, g * HG:(g + 1) * HG],
                                      ident[:, :])
                mm.then_inc(max_t_ready, 1)

            def mask_transposed(b, u, _, bank):
                wait(pe, mask_made, b.count(2, 2))
                half = bank[:, :].bitcast(BF16)
                for mt in (2 * u, 2 * u + 1):
                    for t in range(NT):
                        at = (mt % 2) * N + t * P
                        mm = pe.transpose(half[:, at:at + P], mask[b.parity][:, t, mt * P:(mt + 1) * P], ident_bf[:, :])
                mm.then_inc(mask_t_ready, 1)

            def project_out(b, u, i, bank):
                wait(pe, attn_ready, b.count(2, 2))
                t = 2 * u + i
                for g in range(G):
                    mm = pe.matmul(bank[:, i * D:(i + 1) * D], attn_t[g][:, t * P:(t + 1) * P],
                                   w_sb["o"][:, g, :], start=(g == 0), stop=(g == G - 1))
                if i == 1:
                    mm.then_inc(out_ready, 1)

            jobs = {"x_t": x_transposed, "qk": project_qk, "v": project_v, "max_t": max_transposed,
                    "mask_t": mask_transposed, "out": project_out, "den": denominators}

            def period(b):
                for h in range(H):
                    for t in range(NT):
                        if b.exists:
                            scores_transposed(b, h, t)
                        if b.plus(1).exists:
                            scores(b.plus(1), h, t)
                        job, part, piece, rel = EXTRA[NT * h + t]
                        if b.plus(rel).exists and job == "pv":
                            probs_times_v(b.plus(rel), part, piece)
                        elif b.plus(rel).exists:
                            if piece == 0:
                                wait_short_bank(pe, b, SHORT.index((job, part, rel)))
                            jobs[job](b.plus(rel), part, piece, bank_of(job, part))

            run_periods(pe, period)

        @block.scalar
        def _(act):
            def probs(b, h, t):
                if t == 0 and h in (0, HG - 1, H - 1):
                    wait(act, pv_ready, b.count(2, {0: -1, HG - 1: 0, H - 1: 1}[h]))
                act.wait_ge(scores_t_ready, b.count(TILES, NT * h + t + 1))
                act.activation(probs_t[:, buffer_of(h), t, :], ps_st[(NT * h + t) % ST_BANKS][:, :], ACT.Exp,
                               scale=SCALE).then_inc(probs_ready, 1)

            def seed(b, n):
                if n % NT in SEEDED:
                    if n == 0:
                        act.wait_ge(bits_set, 1)
                        act.wait_ge(mask_t_copied, b.count(2, 2))
                    wait(act, probs_ready, b.count(TILES, bank_before(n) + 1))
                    act.copy(ps_st[n % ST_BANKS][:, :], mask_t[b.parity][:, n % NT, :]).then_inc(mask_seeded, 1)

            def copy_x_t(b, k, bank):
                wait(act, v_ready, b.count(2, -2))
                act.wait_ge(x_t_ready, b.count(2, k + 1))
                act.copy(x_t[b.parity][:, k, :], bank[:, :]).then_inc(x_t_copied, 1)

            def copy_hi(b, u, bank):
                g, prev = u // 2, b.plus(-1)
                wait(act, packs_laid[prev.parity][g], prev.count_of_parity(PACKS, PACKS))
                act.wait_ge(qk_ready, b.count(4, u + 1))
                act.copy(hi[u % 2][g][:, :], bank[:, :]).then_inc(hi_copied, 1)

            def copy_v(b, u, bank):
                wait(act, pv_ready, b.count(2, -2))
                act.wait_ge(v_ready, b.count(2, u + 1))
                act.copy(v_sb[b.parity][:, 2 * u:2 * u + 2, :],
                         bank[:, :].rearrange("p (t d) -> p t d", t=2)).then_inc(v_copied, 1)

            def copy_max(b, g, bank):
                if g == 1:
                    act.wait_ge(max_laid[b.parity][0], b.count_of_parity(16, 16))
                elif b.plus(-1).exists:
                    act.wait_ge(max_laid[b.plus(-1).parity][1], b.plus(-1).count_of_parity(16, 16))
                act.wait_ge(max_t_ready, b.count(2, g + 1))
                act.mul(neg_max[:, :], bank[0:HG, :], -1.0).then_inc(max_copied, 1)

            def copy_mask_t(b, u, bank):
                wait(act, scores_t_ready, b.count(TILES, -TILES))
                act.wait_ge(mask_t_ready, b.count(2, u + 1))
                act.copy(mask_t[b.parity][:, 2 * u:2 * u + 2, :],
                         bank[:, :].bitcast(BF16).rearrange("p (t n) -> p t n", t=2)).then_inc(mask_t_copied, 1)

            jobs = {"x_t": copy_x_t, "qk": copy_hi, "v": copy_v, "max_t": copy_max, "mask_t": copy_mask_t}

            def period(b):
                for h in range(H):
                    for t in range(NT):
                        if b.exists:
                            n = NT * h + t
                            probs(b, h, t)
                            if n + AHEAD < TILES:
                                seed(b, n + AHEAD)
                        if NT * h + t in SCALAR_EXTRA:
                            job, part, rel = SCALAR_EXTRA[NT * h + t]
                            if b.plus(rel).exists:
                                jobs[job](b.plus(rel), part, bank_of(job, part))
                        if b.plus(1).exists and NT * h + t >= TILES - AHEAD:
                            seed(b.plus(1), NT * h + t + AHEAD - TILES)

            run_periods(act, period)

        @block.vector
        def _(dve):
            for p in range(2):
                dve.memset(k_pack[p][ROWS:P, :, :].bitcast(F32), 1.0)
            dve.memset(minus_half[:, :], -0.5)
            dve.memset(ones[:, :], 1.0).then_inc(consts_made, 1)

            def maximum(b, h, t):
                if h == 0 and t == 0:
                    wait(dve, max_t_ready, b.count(2, -2))
                    dve.wait_ge(mask_made, b.count(2, 2))
                wait_apart(dve, scores_ready, b.count(TILES, NT * h + t + 1), dve_passed)
                dve.tensor_tensor_reduce(ps_s[t % 2][:, :], ps_s[t % 2][:, :], mask[b.parity][:, t, :], 1.0, -3.0e38,
                                         ALU.add, ALU.max, row_max[b.parity][:, t, h:h + 1]).then_inc(max_done, 1)

            def make_mask(b, half):
                if half == 0:
                    wait(dve, mask_t_ready, b.count(2, -2))
                dve.wait_ge(adj_loaded, b.count(32, 16 * half + 16))
                dve.tensor_scalar(mask[b.parity][:, 2 * half:2 * half + 2, :], adj_in[:, :, :], 0, MASKED,
                                  ALU.is_equal, ALU.mult).then_inc(mask_made, 1)

            def copy_lo(b, u):
                bank = bank_of("qk", u)
                dve.wait_ge(hi_copied, b.count(4, u + 1))
                dve.tensor_tensor(lo[u % 2][u // 2][:, :], bank[:, :], hi[u % 2][u // 2][:, :].bitcast(F32),
                                  ALU.subtract).then_inc(lo_copied, 1)

            def normalise(b, g):
                dve.wait_ge(pv_ready, b.count(2, g + 1))
                wait(dve, out_ready, b.count(2, 0))
                dve.wait_ge(inv_den_made, b.count(2 * NT, NT * (g + 1)))
                dve.scalar_tensor_tensor(out=attn_t[g][:, :], in0=ps_pv[:, :], scalar=0.0, in1=inv_den[:, :],
                                         op0=ALU.max, op1=ALU.mult).then_inc(attn_ready, 1)

            def invert(b, part):
                g, piece = part
                bank = bank_of("den", g)
                if piece == 0:
                    dve.wait_ge(den_ready, b.count(2, g + 1))
                    wait(dve, attn_ready, b.count(2, g))
                at = slice(piece * P, (piece + 1) * P)
                dve.reciprocal(inv_den[:, at], bank[:, at]).then_inc(inv_den_made, 1)

            def add_residual(b, u):
                dve.wait_ge(residual_loaded, b.count(16, 16))
                dve.wait_ge(out_ready, b.count(2, u + 1))
                rows = y[:, 2 * u:2 * u + 2, :].rearrange("p t d -> p (t d)")
                dve.tensor_tensor(rows, bank_of("out", u)[:, :], rows, ALU.add).then_inc(residual_added, 1)

            def statistics(b, u):
                dve.wait_ge(residual_added, b.count(2, u + 1))
                for t in (2 * u, 2 * u + 1):
                    dve.bn_stats(stats[:, t, :], y[:, t, :]).then_inc(stats_made, 1)

            def mean_and_variance(b, _):
                wait_apart(dve, stats_made, b.count(NT, NT), dve_passed)
                for t in range(NT):
                    ins = dve.bn_aggr(mean_var[:, t, :], stats[:, t, :])
                ins.then_inc(mean_var_made, 1)
                dve.wait_ge(mean_var_made, b.count(1, 1))
                dve.tensor_scalar(var_eps[:, :], mean_var[:, :, 1], EPS, None, ALU.add).then_inc(var_eps_made, 1)

            def normalise_rows(b, _):
                dve.wait_ge(rstd_made, b.count(1, 1))
                for t in range(NT):
                    ins = dve.tensor_scalar(y[:, t, :], y[:, t, :], mean_var[:, t, 0:1],
                                            rstd[:, t:t + 1], ALU.subtract, ALU.mult)
                ins.then_inc(normed, 1)

            jobs = {"mask": make_mask, "inv": invert, "attn": normalise, "qk": copy_lo, "out": add_residual,
                    "stats": statistics, "mean": mean_and_variance, "rows": normalise_rows}

            def period(b):
                for h in range(H):
                    for t in range(NT):
                        if b.plus(1).exists:
                            maximum(b.plus(1), h, t)
                        for after, job, part, rel in VECTOR_EXTRA:
                            if after == NT * h + t and b.plus(rel).exists:
                                jobs[job](b.plus(rel), part)

            run_periods(dve, period)

        @block.gpsimd
        def _(pool):
            for n, idt in enumerate((ident, ident_bf)):
                pool.memset(idt[:, :], 0.0).then_inc(zeroed, 1)
                pool.wait_ge(zeroed, n + 1)
                pool.affine_select(out=idt[:, :], in_=idt[:, :], compare_op=ALU.not_equal, fill=1.0, base=0,
                                   pattern=[[-1, P]], channel_multiplier=1).then_inc(idents_made, 1)
            pool.wait_ge(consts_made, 1)

            def sum_probs(b, h):
                g, i = h // HG, h % HG
                if i == 0:
                    wait(pool, den_ready, b.count(2, g))
                pool.wait_ge(probs_ready, b.count(TILES, NT * (h + 1)))
                total, part = probs_sum[:, i, :], probs_t[:, buffer_of(h), :, :]
                pool.tensor_tensor(total, part[:, 0, :], part[:, 1, :], ALU.add).then_inc(partly_summed, 1)
                pool.wait_ge(partly_summed, b.count(2 * H, 2 * h + 1))
                pool.tensor_tensor(total, total, part[:, 2, :], ALU.add).then_inc(partly_summed, 1)
                pool.wait_ge(partly_summed, b.count(2 * H, 2 * h + 2))
                pool.tensor_tensor(total, total, part[:, 3, :], ALU.add).then_inc(probs_summed, 1)

            def period(b):
                last = b.plus(-1)
                for h in range(H):
                    if b.exists:
                        sum_probs(b, h)
                    if h == 4 and last.exists:
                        pool.wait_ge(var_eps_made, last.count(1, 1))
                        pool.tensor_tensor(rstd[:, :], var_eps[:, :], minus_half[:, :], ALU.pow).then_inc(rstd_made, 1)

            run_periods(pool, period)


def kernel(x, adj, L0_gnn_Wq, L0_gnn_Wk, L0_gnn_Wv, L0_gnn_Wo):
    import numpy as np
    import concourse.bacc as bacc
    from concourse.bass_utils import run_bass_kernel_spmd

    nc = bacc.Bacc("TRN2", target_bir_lowering=False, num_devices=1)
    arrays = {"in_x": x, "in_adj": adj, "in_wq": L0_gnn_Wq, "in_wk": L0_gnn_Wk, "in_wv": L0_gnn_Wv, "in_wo": L0_gnn_Wo}
    for name in ("in_wq", "in_wk"):
        arrays[name] = np.asarray(arrays[name]).reshape(D, G, HG, DK).transpose(0, 1, 3, 2).reshape(D, D)
    arrays = {name: np.ascontiguousarray(a) for name, a in arrays.items()}
    ins = [nc.dram_tensor(name, a.shape, mybir.dt.from_np(a.dtype), kind="ExternalInput").ap()
           for name, a in arrays.items()]
    out = nc.dram_tensor("out", (B, N, D), F32, kind="ExternalOutput").ap()
    graph_attention(nc, *ins, out)
    result = run_bass_kernel_spmd(nc, [arrays], core_ids=[0])
    return result.results[0]["out"]
```

```python
from contextlib import ExitStack

import concourse.bass as bass
from concourse import mybir

F32 = mybir.dt.float32
F32R = mybir.dt.float32r
BF16 = mybir.dt.bfloat16
I32 = mybir.dt.int32
ALU = mybir.AluOpType
ACT = mybir.ActivationFunctionType

B, N, D, H = 16, 512, 256, 8
DK = D // H
P = 128
NT = N // P
KT = D // P
HG = P // DK
G = H // HG
TILES = H * NT
ROWS = 3 * DK
SCALE = 1.0 / float(DK) ** 0.5
MASKED = -1.0e30
EPS = 1e-5
PACKS = 6 * 16
SEEDED = (0, 1, 3, 4, 5)
AHEAD = 2
ST_BANKS = 3
WARM_UP = 20
FIRST, LAST = -3, B
LEAD = 10
LOOP_FROM, LOOP_TO = 2, B - 4


class Batch:

    def __init__(self, off, j=None, low=0):
        self.off, self.j, self.low = off, j, low

    def plus(self, n):
        return Batch(self.off + n, self.j, self.low)

    @property
    def parity(self):
        return self.off % 2

    @property
    def exists(self):
        return self.j is not None or 0 <= self.off < B

    def count(self, per_batch, k):
        if self.j is None:
            return self.off * per_batch + k
        assert 2 * self.low * per_batch + self.off * per_batch + k > 0
        return self.j * (2 * per_batch) + (self.off * per_batch + k)

    def count_of_parity(self, per_batch, k):
        if self.j is None:
            return (self.off // 2) * per_batch + k
        assert (self.low + self.off // 2) * per_batch + k > 0
        return self.j * per_batch + ((self.off // 2) * per_batch + k)

    @property
    def index(self):
        return self.off if self.j is None else self.j * 2 + self.off


def tile_at(b, n):
    return b.plus(n // TILES), n % TILES


def timed(table, b):
    def held_back(line):
        return table is not EXTRA and line[1] == "qk" and line[2] >= 2 and line[-1] == 2

    if b.j is None and b.off == -2:
        return [line for line in table if not held_back(line)]
    if b.j is None and b.off == -1:
        early = [(-1,) + line[1:] for line in table if (line[1], line[-1]) in EARLY]
        back = [(2 * line[2] - 4,) + line[1:-1] + (1,) for line in table if held_back(line)]
        return sorted(early + back + [line for line in table if (line[1], line[-1]) not in EARLY],
                      key=lambda line: line[0])
    return table


def wait(eng, sem, value):
    if not isinstance(value, int) or value > 0:
        eng.wait_ge(sem, value)


def wait_apart(eng, sem, value, passed):
    if not isinstance(value, int) or value > 0:
        eng.wait_ge(sem, value).then_inc(passed, 1)


def run_periods(eng, period):
    for b in range(FIRST, LOOP_FROM):
        period(Batch(b))
    with eng.Fori(LOOP_FROM // 2, LOOP_TO // 2) as j:
        for off in range(2):
            period(Batch(off, j, LOOP_FROM // 2))
    for b in range(LOOP_TO, LAST + 1):
        period(Batch(b))


EARLY = (("x_t", 2), ("mask_t", 1), ("v", 1))
SYNC_JOBS = [("pack", 0, 1), ("x", 1, 2), ("max", 1, 0), ("adj", 1, 2), ("pack", 1, 1), ("max", 0, 1), ("adj", 0, 3),
             ("x", 0, 3), ("store", 0, -1), ("residual", 0, 0)]
EXTRA = [(1, "max_t", 1, 0, 0), (2, "x_t", 0, 0, 2), (3, "mask_t", 0, 0, 1), (5, "out", 0, 0, -1),
         (6, "out", 0, 1, -1), (6, "x_t", 1, 0, 2), (8, "out", 1, 0, -1), (9, "out", 1, 1, -1),
         (9, "mask_t", 1, 0, 1), (11, "den", 0, 0, 0), (11, "qk", 0, 0, 2), (12, "qk", 0, 1, 2), (13, "pv", 0, 0, 0),
         (13, "pv", 0, 1, 0), (14, "pv", 0, 2, 0), (16, "pv", 0, 3, 0), (17, "max_t", 0, 0, 1), (18, "qk", 1, 0, 2),
         (18, "qk", 1, 1, 2), (19, "v", 0, 0, 1), (20, "v", 0, 1, 1), (21, "v", 1, 0, 1), (23, "v", 1, 1, 1),
         (24, "pv", 1, 0, 0), (26, "den", 1, 0, 0), (28, "pv", 1, 1, 0), (28, "pv", 1, 2, 0), (29, "qk", 2, 0, 2),
         (30, "pv", 1, 3, 0), (31, "qk", 2, 1, 2), (31, "qk", 3, 0, 2), (31, "qk", 3, 1, 2)]
SHORT = [(job, part, rel) for _, job, part, piece, rel in EXTRA if job != "pv" and piece == 0]
SCALAR_EXTRA = [(1, "max_t", 1, 0), (2, "x_t", 0, 2), (3, "mask_t", 0, 1), (6, "x_t", 1, 2), (9, "mask_t", 1, 1),
                (12, "qk", 0, 2), (17, "max_t", 0, 1), (18, "qk", 1, 2), (21, "v", 0, 1), (28, "v", 1, 1),
                (31, "qk", 2, 2), (31, "qk", 3, 2)]
GPSIMD_EXTRA = [(13, "rstd", 0, -1)]
VECTOR_EXTRA = [(1, "mask", 0, 2), (1, "attn", 1, -1), (3, "x_t", 0, 2), (6, "out", 0, -1), (7, "x_t", 1, 2),
                (8, "stats", 0, -1), (9, "out", 1, -1), (10, "stats", 1, -1), (10, "mean", 0, -1),
                (11, "inv", (0, 0), 0), (12, "inv", (0, 1), 0), (13, "inv", (0, 2), 0), (13, "qk", 0, 2),
                (14, "inv", (0, 3), 0), (17, "mask", 1, 2), (17, "attn", 0, 0), (18, "rows", 0, -1),
                (19, "qk", 1, 2), (26, "inv", (1, 0), 0), (27, "inv", (1, 1), 0), (28, "inv", (1, 2), 0),
                (29, "inv", (1, 3), 0), (31, "qk", 2, 2), (31, "qk", 3, 2)]


def graph_attention(nc, x, adj, wq, wk, wv, wo, out):
    with ExitStack() as ctx:
        def sb(name, shape, dt):
            return ctx.enter_context(nc.sbuf_tensor(name, shape, dt))

        def psum(name):
            return ctx.enter_context(nc.psum_tensor(name, [P, 512], F32))

        def sem(name):
            return ctx.enter_context(nc.semaphore(name))

        w_o = sb("w_o", [P, KT, D], F32)
        w_hi = {n: sb(f"w_hi_{n}", [P, KT, D], F32R) for n in "qkv"}
        w_lo = {n: sb(f"w_lo_{n}", [P, KT, D], F32R) for n in "qkv"}
        ident = sb("ident", [P, P], F32)
        ident_bf = sb("ident_bf", [P, P], BF16)
        ones = sb("ones", [P, DK], F32)
        minus_half = sb("minus_half", [P, NT], F32)
        x_in = sb("x_in", [P, NT // 2, D], F32)
        adj_in = sb("adj_in", [P, NT // 2, N], I32)
        y = sb("y", [P, NT, D], F32)
        mask = [sb(f"mask{p}", [P, NT, N], BF16) for p in range(2)]
        mask_t = [sb(f"mask_t{p}", [P, NT, N], BF16) for p in range(2)]
        x_hi = [sb(f"x_hi{p}", [P, KT, N], F32R) for p in range(2)]
        x_lo = [sb(f"x_lo{p}", [P, KT, N], F32R) for p in range(2)]
        hi = [sb(f"hi_{n}", [P, N], F32R) for n in "qk"]
        lo = [sb(f"lo_{n}", [P, N], F32R) for n in "qk"]
        q_pack = [sb(f"q_pack{p}", [P, H, N], F32R) for p in range(2)]
        k_pack = [sb(f"k_pack{p}", [P, H, N], F32R) for p in range(2)]
        v_sb = [sb(f"v_sb{p}", [P, NT, D], F32) for p in range(2)]
        row_max = [sb(f"row_max{p}", [P, NT, H], F32) for p in range(2)]
        probs_t = sb("probs_t", [P, H - 1, NT, N], F32)
        probs_sum = sb("probs_sum", [P, HG, N], F32)
        attn_t = [sb(f"attn_t{g}", [P, N], F32) for g in range(G)]
        stats = sb("stats", [P, NT, 6], F32)
        mean_var = sb("mean_var", [P, NT, 2], F32)
        var_eps = sb("var_eps", [P, NT], F32)
        rstd = sb("rstd", [P, NT], F32)

        ps_s = [psum(f"ps_s{i}") for i in range(2)]
        ps_st = [psum(f"ps_st{i}") for i in range(ST_BANKS)]
        ps_pv = psum("ps_pv")
        ps_short = [psum(f"ps_short{i}") for i in range(2)]

        w_loaded = {n: sem(f"w_{n}_loaded") for n in "qkvo"}
        x_loaded = [sem(f"x_loaded{i}") for i in range(2)]
        adj_loaded = sem("adj_loaded")
        residual_loaded = sem("residual_loaded")
        packs_laid = [[sem(f"packs_laid{p}{g}") for g in range(G)] for p in range(2)]
        max_laid = [[sem(f"max_laid{p}{g}") for g in range(G)] for p in range(2)]
        out_stored = sem("out_stored")
        bits_set = sem("bits_set")
        x_t_ready = sem("x_t_ready")
        qk_ready = sem("qk_ready")
        max_t_ready = sem("max_t_ready")
        mask_t_ready = sem("mask_t_ready")
        v_ready = sem("v_ready")
        out_ready = sem("out_ready")
        scores_ready = sem("scores_ready")
        scores_t_ready = sem("scores_t_ready")
        den_ready = sem("den_ready")
        pv_ready = sem("pv_ready")
        mask_seeded = sem("mask_seeded")
        w_hi_made = sem("w_hi_made")
        x_hi_copied = sem("x_hi_copied")
        hi_copied = sem("hi_copied")
        max_copied = sem("max_copied")
        mask_t_copied = sem("mask_t_copied")
        v_copied = sem("v_copied")
        probs_ready = sem("probs_ready")
        consts_made = sem("consts_made")
        mask_made = sem("mask_made")
        w_lo_made = sem("w_lo_made")
        x_lo_copied = sem("x_lo_copied")
        lo_copied = sem("lo_copied")
        max_done = sem("max_done")
        inv_den_made = sem("inv_den_made")
        attn_ready = sem("attn_ready")
        residual_added = sem("residual_added")
        stats_made = sem("stats_made")
        mean_var_made = sem("mean_var_made")
        var_eps_made = sem("var_eps_made")
        normed = sem("normed")
        dve_passed = sem("dve_passed")
        sp_passed = sem("sp_passed")
        zeroed = sem("zeroed")
        idents_made = sem("idents_made")
        ones_row_made = sem("ones_row_made")
        partly_summed = sem("partly_summed")
        probs_summed = sem("probs_summed")
        rstd_made = sem("rstd_made")

        def seeds_before(n):
            return sum(i % (2 * NT) in SEEDED for i in range(n))

        def buffer_of(h):
            return h if h < H - 1 else HG - 1

        def bank_before(n):
            return n - ST_BANKS if n >= ST_BANKS else (TILES - 1 - (TILES - 1 - n) % ST_BANKS) - TILES

        x_v = x.rearrange("b (t p) d -> b p t d", p=P)
        adj_v = adj.rearrange("b (t p) m -> b p t m", p=P)
        out_v = out.rearrange("b (t p) d -> b p t d", p=P)

        SHORT_READ = {"x_t": (x_lo_copied, 2), "qk": (lo_copied, 4), "max_t": (max_copied, 2),
                      "mask_t": (mask_t_copied, 2), "v": (v_copied, 2), "out": (residual_added, 2),
                      "den": (inv_den_made, 2 * NT)}

        def among_first(b):
            return b.j is None and b.off < 2

        def x_in_of(b, half):
            return y[:, 2 - 2 * b.off:4 - 2 * b.off, :] if half == 1 and among_first(b) else x_in[:, :, :]

        def sums_alone(b, g):
            return b.j is None and b.off == B - 1 and g == G - 1

        def bank_number(job, part):
            return [(j, p) for j, p, _ in SHORT].index((job, part)) % 2

        def own_bank(job, b):
            return job == "qk" and b.j is None and b.off == 0

        def bank_of(job, part, b):
            if own_bank(job, b):
                return (ps_s[0], ps_s[1], ps_pv, ps_st[0])[part]
            return ps_short[bank_number(job, part)]

        def wait_short_bank(eng, b, job, part, rel):
            if own_bank(job, b.plus(rel)):
                return
            period, bank = b, bank_number(job, part)
            while period.j is not None or period.off > FIRST:
                in_bank = [(j, p, r) for _, j, p, piece, r in timed(EXTRA, period)
                           if (j, p, r) in SHORT and piece == 0 and bank_number(j, p) == bank
                           and period.plus(r).exists and not own_bank(j, period.plus(r))]
                if period is b:
                    in_bank = in_bank[:in_bank.index((job, part, rel))]
                if in_bank:
                    job, part, rel = in_bank[-1]
                    s, per = SHORT_READ[job]
                    each = NT if job == "den" else 1
                    wait(eng, s, period.plus(rel).count(per, each * (part + 1)))
                    return
                period = period.plus(-1)

        block = ctx.enter_context(nc.Block())

        @block.sync
        def _(sp):
            def lay_out(b, g):
                wait_apart(sp, scores_t_ready, b.count(TILES, NT * HG * (g + 1) - 2 * TILES), sp_passed)
                for i, (pack, srcs) in enumerate(((q_pack, (hi[0], lo[0], hi[0])), (k_pack, (hi[1], hi[1], lo[1])))):
                    wait_apart(sp, lo_copied, b.count(4, 2 * g + i + 1), sp_passed)
                    for c, src in enumerate(srcs):
                        sp.dma_start(pack[b.parity][c * DK:(c + 1) * DK, g * HG:(g + 1) * HG, :].bitcast(F32),
                                     src[:, :].bitcast(F32)).then_inc(packs_laid[b.parity][g], 16)

            def lay_out_max(b, g):
                wait_apart(sp, max_copied, b.count(2, g + 1), sp_passed)
                pack = q_pack[b.parity]
                sp.dma_start(pack[ROWS:ROWS + 1, g * HG + 1:(g + 1) * HG, :].bitcast(F32),
                             pack[ROWS + 1:ROWS + HG, g * HG, :].bitcast(F32)).then_inc(max_laid[b.parity][g], 16)

            def load_x(b, half):
                if half == 0 or not among_first(b):
                    wait_apart(sp, x_t_ready, b.count(2, half), sp_passed)
                sp.dma_start(x_in_of(b, half), x_v[b.index, :, 2 * half:2 * half + 2, :]).then_inc(x_loaded[half], 16)

            def load_adj(b, half):
                wait_apart(sp, mask_made, b.count(2, half), sp_passed)
                sp.dma_start(adj_in[:, :, :], adj_v[b.index, :, 2 * half:2 * half + 2, :]).then_inc(adj_loaded, 16)

            def load_residual(b, _):
                wait_apart(sp, out_stored, b.count(16, 0), sp_passed)
                sp.dma_start(y[:, :, :], x_v[b.index]).then_inc(residual_loaded, 16)

            def store(b, _):
                wait_apart(sp, normed, b.count(1, 1), sp_passed)
                sp.dma_start(out_v[b.index], y[:, :, :]).then_inc(out_stored, 16)

            jobs = {"x": load_x, "adj": load_adj, "pack": lay_out, "max": lay_out_max, "residual": load_residual,
                    "store": store}

            def period(b):
                if b.off == FIRST + 1:
                    load_x(Batch(1), 0)
                    load_x(Batch(1), 1)
                for job, part, rel in SYNC_JOBS:
                    if b.plus(rel).exists and not (job == "x" and among_first(b.plus(rel))):
                        jobs[job](b.plus(rel), part)

            load_x(Batch(0), 0)
            load_x(Batch(0), 1)
            run_periods(sp, period)
            sp.wait_ge(out_stored, 16 * B)

        @block.tensor
        def _(pe):
            pe.wait_ge(idents_made, 2)
            pe.wait_ge(consts_made, 1)
            for bank in ps_st:
                for t in range(NT):
                    mm = pe.matmul(bank[:, t * P:(t + 1) * P], ident_bf[:, :], ident_bf[:, :], start=(t == 0),
                                   stop=(t == NT - 1), skip_group_check=True)
            mm.then_inc(bits_set, 1)
            for _ in range(WARM_UP):
                pe.matmul(ps_pv[:, 0:P], ident_bf[:, :], ident_bf[:, :], start=True, stop=True)

            def scores(b, h, t):
                if h % HG == 0 and t == 0:
                    wait(pe, packs_laid[b.parity][h // HG], b.count_of_parity(PACKS, PACKS))
                wait(pe, max_done, b.count(TILES, NT * h + t - 1))
                pe.matmul(ps_s[t % 2][:, :], q_pack[b.parity][0:ROWS, h, t * P:(t + 1) * P],
                          k_pack[b.parity][0:ROWS, h, :], start=True, stop=True).then_inc(scores_ready, 1)

            def scores_transposed(b, h, t):
                if h % HG == 0 and t == 0:
                    wait(pe, max_laid[b.parity][h // HG], b.count_of_parity(16, 16))
                    if b.j is None and b.off < 2:
                        pe.wait_ge(ones_row_made, b.off + 1)
                n = NT * h + t
                bank, seeded = ps_st[n % ST_BANKS], seeds_before(n + 1) > seeds_before(n)
                if seeded:
                    pe.wait_ge(mask_seeded, b.count(seeds_before(TILES), seeds_before(n + 1)))
                else:
                    wait(pe, probs_ready, b.count(TILES, bank_before(n) + 1))
                    if h == 0:
                        pe.wait_ge(mask_t_copied, b.count(2, 2))
                mm = pe.matmul(bank[:, :], k_pack[b.parity][0:ROWS + 1, h, t * P:(t + 1) * P],
                               q_pack[b.parity][0:ROWS + 1, h, :], start=not seeded, stop=seeded, skip_group_check=True)
                if not seeded:
                    mm = pe.matmul(bank[:, :], ident_bf[:, :], mask_t[b.parity][:, t, :], start=False, stop=True,
                                   skip_group_check=True)
                mm.then_inc(scores_t_ready, 1)

            def probs_times_v(b, g, t):
                if t == 0:
                    wait(pe, probs_ready, b.count(TILES, NT * HG * (g + 1)))
                    wait(pe, v_copied, b.count(2, 2))
                    wait(pe, attn_ready, b.count(2, g))
                for i in range(HG):
                    h = g * HG + i
                    mm = pe.matmul(ps_pv[i * DK:(i + 1) * DK, :], v_sb[b.parity][:, t, h * DK:(h + 1) * DK],
                                   probs_t[:, buffer_of(h), t, :], start=(t == 0), stop=(t == NT - 1))
                if t == NT - 1:
                    mm.then_inc(pv_ready, 1)

            def denominators(b, g, _, bank):
                if sums_alone(b, g):
                    wait(pe, probs_ready, b.count(TILES, NT * HG * (g + 1)))
                    tiles = [[probs_t[:, buffer_of(g * HG + i), t, :] for i in range(HG)] for t in range(NT)]
                else:
                    wait(pe, probs_summed, b.count(H, HG * (g + 1)))
                    tiles = [[probs_sum[:, i, :] for i in range(HG)]]
                for t, heads in enumerate(tiles):
                    for i, tile in enumerate(heads):
                        mm = pe.matmul(bank[i * DK:(i + 1) * DK, :], ones[:, :], tile,
                                       start=(t == 0), stop=(t == len(tiles) - 1))
                mm.then_inc(den_ready, 1)

            def x_transposed(b, u, _, bank):
                pe.wait_ge(x_loaded[u], b.count(16, 16))
                for k in range(KT):
                    for i in range(2):
                        at = (2 * k + i) * P
                        mm = pe.transpose(bank[:, at:at + P], x_in_of(b, u)[:, i, k * P:(k + 1) * P], ident[:, :])
                mm.then_inc(x_t_ready, 1)

            def project_qk(b, u, k, bank):
                wait(pe, x_lo_copied, b.count(2, 2))
                if b.j is None and b.off == 0 and u < 2:
                    pe.wait_ge(w_lo_made, u + 1)
                n, cols = "qk"[u % 2], slice(u // 2 * P, (u // 2 + 1) * P)
                for i, (w, xt) in enumerate(((w_hi, x_hi), (w_hi, x_lo), (w_lo, x_hi))):
                    mm = pe.matmul(bank[:, :], w[n][:, k, cols], xt[b.parity][:, k, :],
                                   start=(k == 0 and i == 0), stop=(k == KT - 1 and i == 2))
                if k == KT - 1:
                    mm.then_inc(qk_ready, 1)

            def project_v(b, u, i, bank):
                wait(pe, x_lo_copied, b.count(2, 2))
                if b.j is None and b.off == 0:
                    pe.wait_ge(w_lo_made, 3)
                at = slice((2 * u + i) * P, (2 * u + i + 1) * P)
                for k in range(KT):
                    for p, (xt, w) in enumerate(((x_hi, w_hi), (x_hi, w_lo), (x_lo, w_hi))):
                        mm = pe.matmul(bank[:, i * D:(i + 1) * D], xt[b.parity][:, k, at], w["v"][:, k, :],
                                       start=(k == 0 and p == 0), stop=(k == KT - 1 and p == 2))
                if i == 1:
                    mm.then_inc(v_ready, 1)

            def max_transposed(b, g, _, bank):
                wait(pe, max_done, b.count(TILES, NT * HG * (g + 1)))
                for t in range(NT):
                    mm = pe.transpose(bank[0:HG, t * P:(t + 1) * P], row_max[b.parity][:, t, g * HG:(g + 1) * HG],
                                      ident[:, :])
                mm.then_inc(max_t_ready, 1)

            def mask_transposed(b, u, _, bank):
                wait(pe, mask_made, b.count(2, 2))
                half = bank[:, :].bitcast(BF16)
                for mt in (2 * u, 2 * u + 1):
                    for t in range(NT):
                        at = (mt % 2) * N + t * P
                        mm = pe.transpose(half[:, at:at + P], mask[b.parity][:, t, mt * P:(mt + 1) * P], ident_bf[:, :])
                mm.then_inc(mask_t_ready, 1)

            def project_out(b, u, i, bank):
                wait(pe, attn_ready, b.count(2, 2))
                if b.j is None and b.off == 0:
                    pe.wait_ge(w_loaded["o"], 16)
                t = 2 * u + i
                for g in range(G):
                    mm = pe.matmul(bank[:, i * D:(i + 1) * D], attn_t[g][:, t * P:(t + 1) * P],
                                   w_o[:, g, :], start=(g == 0), stop=(g == G - 1))
                if i == 1:
                    mm.then_inc(out_ready, 1)

            jobs = {"x_t": x_transposed, "qk": project_qk, "v": project_v, "max_t": max_transposed,
                    "mask_t": mask_transposed, "out": project_out, "den": denominators}

            def period(b):
                for pos in range(-1, TILES):
                    batch, n = tile_at(b, pos + LEAD)
                    if batch.exists and pos >= 0:
                        scores_transposed(batch, n // NT, n % NT)
                    if b.plus(1).exists and pos >= 0:
                        scores(b.plus(1), pos // NT, pos % NT)
                    for after, job, part, piece, rel in timed(EXTRA, b):
                        batch = b.plus(rel)
                        if after != pos or not batch.exists:
                            continue
                        if job == "pv":
                            probs_times_v(batch, part, piece)
                            continue
                        if piece == 0:
                            wait_short_bank(pe, b, job, part, rel)
                        jobs[job](batch, part, piece, bank_of(job, part, batch))

            run_periods(pe, period)

        @block.scalar
        def _(act):
            for i, (n, w) in enumerate(zip("qkvo", (wq, wk, wv, wo))):
                w_to = probs_t[:, 0, i, :].rearrange("p (k n) -> p k n", k=KT) if n in "qkv" else w_o[:, :, :]
                act.dma_start(w_to, w.rearrange("(k p) n -> p k n", p=P)).then_inc(w_loaded[n], 16)

            def split_weights(i):
                act.wait_ge(w_loaded["qkv"[i]], 16)
                act.copy(w_hi["qkv"[i]][:, :, :], probs_t[:, 0, i, :].rearrange("p (k n) -> p k n", k=KT)
                         ).then_inc(w_hi_made, 1)

            split_weights(0)
            split_weights(1)

            def probs(b, h, t):
                if t == 0 and h in (0, HG - 1, H - 1):
                    wait(act, pv_ready, b.count(2, {0: -1, HG - 1: 0, H - 1: 1}[h]))
                act.wait_ge(scores_t_ready, b.count(TILES, NT * h + t + 1))
                act.activation(probs_t[:, buffer_of(h), t, :], ps_st[(NT * h + t) % ST_BANKS][:, :], ACT.Exp,
                               scale=SCALE).then_inc(probs_ready, 1)

            def seed(b, n):
                if seeds_before(n + 1) > seeds_before(n):
                    if n == 0:
                        act.wait_ge(bits_set, 1)
                        act.wait_ge(mask_t_copied, b.count(2, 2))
                    wait(act, probs_ready, b.count(TILES, bank_before(n) + 1))
                    act.copy(ps_st[n % ST_BANKS][:, :], mask_t[b.parity][:, n % NT, :]).then_inc(mask_seeded, 1)

            def copy_x_hi(b, u, bank):
                wait(act, qk_ready, b.count(4, -4))
                wait(act, v_ready, b.count(2, -2))
                act.wait_ge(x_t_ready, b.count(2, u + 1))
                act.copy(x_hi[b.parity][:, :, 2 * u * P:2 * (u + 1) * P],
                         bank[:, :].rearrange("p (k n) -> p k n", k=KT)).then_inc(x_hi_copied, 1)

            def copy_hi(b, u, bank):
                if u >= 2:
                    act.wait_ge(packs_laid[b.parity][0], b.count_of_parity(PACKS, PACKS))
                elif b.plus(-1).exists:
                    act.wait_ge(packs_laid[b.plus(-1).parity][1], b.plus(-1).count_of_parity(PACKS, PACKS))
                act.wait_ge(qk_ready, b.count(4, u + 1))
                act.copy(hi[u % 2][:, :], bank[:, :]).then_inc(hi_copied, 1)

            def copy_v(b, u, bank):
                wait(act, pv_ready, b.count(2, -2))
                act.wait_ge(v_ready, b.count(2, u + 1))
                act.copy(v_sb[b.parity][:, 2 * u:2 * u + 2, :],
                         bank[:, :].rearrange("p (t d) -> p t d", t=2)).then_inc(v_copied, 1)

            def copy_max(b, g, bank):
                act.wait_ge(max_t_ready, b.count(2, g + 1))
                act.mul(q_pack[b.parity][ROWS:ROWS + HG, g * HG, :], bank[0:HG, :], -1.0).then_inc(max_copied, 1)

            def copy_mask_t(b, u, bank):
                wait(act, scores_t_ready, b.count(TILES, -TILES))
                act.wait_ge(mask_t_ready, b.count(2, u + 1))
                act.copy(mask_t[b.parity][:, 2 * u:2 * u + 2, :],
                         bank[:, :].bitcast(BF16).rearrange("p (t n) -> p t n", t=2)).then_inc(mask_t_copied, 1)

            jobs = {"x_t": copy_x_hi, "qk": copy_hi, "v": copy_v, "max_t": copy_max, "mask_t": copy_mask_t}

            def period(b):
                if b.j is None and b.off == -1:
                    split_weights(2)
                for pos in range(-1, TILES):
                    batch, n = tile_at(b, pos + LEAD)
                    if batch.exists and pos >= 0:
                        probs(batch, n // NT, n % NT)
                    batch, n = tile_at(b, pos + LEAD + AHEAD)
                    if batch.exists and pos >= 0:
                        seed(batch, n)
                    for after, job, part, rel in timed(SCALAR_EXTRA, b):
                        if after == pos and b.plus(rel).exists:
                            jobs[job](b.plus(rel), part, bank_of(job, part, b.plus(rel)))

            run_periods(act, period)

        @block.vector
        def _(dve):
            dve.memset(minus_half[:, :], -0.5)
            dve.memset(ones[:, :], 1.0).then_inc(consts_made, 1)

            def split_weights(i):
                dve.wait_ge(w_hi_made, i + 1)
                dve.tensor_tensor(w_lo["qkv"[i]][:, :, :], probs_t[:, 0, i, :].rearrange("p (k n) -> p k n", k=KT),
                                  w_hi["qkv"[i]][:, :, :].bitcast(F32), ALU.subtract).then_inc(w_lo_made, 1)

            split_weights(0)
            split_weights(1)

            def maximum(b, h, t):
                if h == 0 and t == 0:
                    wait(dve, max_t_ready, b.count(2, -2))
                    dve.wait_ge(mask_made, b.count(2, 2))
                wait_apart(dve, scores_ready, b.count(TILES, NT * h + t + 1), dve_passed)
                dve.tensor_tensor_reduce(ps_s[t % 2][:, :], ps_s[t % 2][:, :], mask[b.parity][:, t, :], 1.0, -3.0e38,
                                         ALU.add, ALU.max, row_max[b.parity][:, t, h:h + 1]).then_inc(max_done, 1)

            def make_mask(b, half):
                if half == 0:
                    wait(dve, mask_t_ready, b.count(2, -2))
                dve.wait_ge(adj_loaded, b.count(32, 16 * half + 16))
                dve.tensor_scalar(mask[b.parity][:, 2 * half:2 * half + 2, :], adj_in[:, :, :], 0, MASKED,
                                  ALU.is_equal, ALU.mult).then_inc(mask_made, 1)

            def copy_x_lo(b, u):
                dve.wait_ge(x_hi_copied, b.count(2, u + 1))
                half = slice(2 * u * P, 2 * (u + 1) * P)
                x_t = bank_of("x_t", u, b)[:, :].rearrange("p (k n) -> p k n", k=KT)
                dve.tensor_tensor(x_lo[b.parity][:, :, half], x_t,
                                  x_hi[b.parity][:, :, half].bitcast(F32), ALU.subtract).then_inc(x_lo_copied, 1)

            def copy_lo(b, u):
                bank = bank_of("qk", u, b)
                dve.wait_ge(hi_copied, b.count(4, u + 1))
                dve.tensor_tensor(lo[u % 2][:, :], bank[:, :], hi[u % 2][:, :].bitcast(F32),
                                  ALU.subtract).then_inc(lo_copied, 1)

            def normalise(b, g):
                dve.wait_ge(pv_ready, b.count(2, g + 1))
                dve.wait_ge(inv_den_made, b.count(2 * NT, NT * (g + 1)))
                dve.scalar_tensor_tensor(out=attn_t[g][:, :], in0=ps_pv[:, :], scalar=0.0, in1=attn_t[g][:, :],
                                         op0=ALU.max, op1=ALU.mult).then_inc(attn_ready, 1)

            def invert(b, part):
                g, piece = part
                bank = bank_of("den", g, b)
                if piece == 0:
                    dve.wait_ge(den_ready, b.count(2, g + 1))
                    wait(dve, out_ready, b.count(2, 0))
                at = slice(piece * P, (piece + 1) * P)
                dve.reciprocal(attn_t[g][:, at], bank[:, at]).then_inc(inv_den_made, 1)

            def add_residual(b, u):
                dve.wait_ge(residual_loaded, b.count(16, 16))
                dve.wait_ge(out_ready, b.count(2, u + 1))
                rows = y[:, 2 * u:2 * u + 2, :].rearrange("p t d -> p (t d)")
                dve.tensor_tensor(rows, bank_of("out", u, b)[:, :], rows, ALU.add).then_inc(residual_added, 1)

            def statistics(b, u):
                dve.wait_ge(residual_added, b.count(2, u + 1))
                for t in (2 * u, 2 * u + 1):
                    dve.bn_stats(stats[:, t, :], y[:, t, :]).then_inc(stats_made, 1)

            def mean_and_variance(b, _):
                wait_apart(dve, stats_made, b.count(NT, NT), dve_passed)
                for t in range(NT):
                    ins = dve.bn_aggr(mean_var[:, t, :], stats[:, t, :])
                ins.then_inc(mean_var_made, 1)
                dve.wait_ge(mean_var_made, b.count(1, 1))
                dve.tensor_scalar(var_eps[:, :], mean_var[:, :, 1], EPS, None, ALU.add).then_inc(var_eps_made, 1)

            def normalise_rows(b, _):
                dve.wait_ge(rstd_made, b.count(1, 1))
                for t in range(NT):
                    ins = dve.tensor_scalar(y[:, t, :], y[:, t, :], mean_var[:, t, 0:1],
                                            rstd[:, t:t + 1], ALU.subtract, ALU.mult)
                ins.then_inc(normed, 1)

            jobs = {"mask": make_mask, "inv": invert, "attn": normalise, "x_t": copy_x_lo, "qk": copy_lo,
                    "out": add_residual, "stats": statistics, "mean": mean_and_variance, "rows": normalise_rows}

            def period(b):
                if b.j is None and b.off == -1:
                    split_weights(2)
                for pos in range(-1, TILES):
                    if b.plus(1).exists and pos >= 0:
                        maximum(b.plus(1), pos // NT, pos % NT)
                    for after, job, part, rel in timed(VECTOR_EXTRA, b):
                        if after == pos and b.plus(rel).exists:
                            jobs[job](b.plus(rel), part)

            run_periods(dve, period)

        @block.gpsimd
        def _(pool):
            for n, idt in enumerate((ident, ident_bf)):
                pool.memset(idt[:, :], 0.0).then_inc(zeroed, 1)
                pool.wait_ge(zeroed, n + 1)
                pool.affine_select(out=idt[:, :], in_=idt[:, :], compare_op=ALU.not_equal, fill=1.0, base=0,
                                   pattern=[[-1, P]], channel_multiplier=1).then_inc(idents_made, 1)
            for p in range(2):
                pool.wait_ge(idents_made if p == 0 else ones_row_made, 2 - p)
                pool.memset(k_pack[p][ROWS:P, :, :].bitcast(F32), 1.0).then_inc(ones_row_made, 1)
            pool.wait_ge(ones_row_made, 2)
            pool.wait_ge(consts_made, 1)

            def sum_probs(b, h):
                g, i = h // HG, h % HG
                if i == 0:
                    wait(pool, den_ready, b.count(2, g))
                pool.wait_ge(probs_ready, b.count(TILES, NT * (h + 1)))
                total, part = probs_sum[:, i, :], probs_t[:, buffer_of(h), :, :]
                pool.tensor_tensor(total, part[:, 0, :], part[:, 1, :], ALU.add).then_inc(partly_summed, 1)
                pool.wait_ge(partly_summed, b.count(2 * H, 2 * h + 1))
                pool.tensor_tensor(total, total, part[:, 2, :], ALU.add).then_inc(partly_summed, 1)
                pool.wait_ge(partly_summed, b.count(2 * H, 2 * h + 2))
                pool.tensor_tensor(total, total, part[:, 3, :], ALU.add).then_inc(probs_summed, 1)

            def reciprocal_std(b, _):
                pool.wait_ge(var_eps_made, b.count(1, 1))
                pool.tensor_tensor(rstd[:, :], var_eps[:, :], minus_half[:, :], ALU.pow).then_inc(rstd_made, 1)

            jobs = {"rstd": reciprocal_std}

            def period(b):
                for pos in range(-1, TILES):
                    batch, n = tile_at(b, pos + LEAD)
                    if batch.exists and n % NT == 0 and pos >= 0 and not sums_alone(batch, n // NT // HG):
                        sum_probs(batch, n // NT)
                    for after, job, part, rel in timed(GPSIMD_EXTRA, b):
                        if after == pos and b.plus(rel).exists:
                            jobs[job](b.plus(rel), part)

            run_periods(pool, period)


def kernel(x, adj, L0_gnn_Wq, L0_gnn_Wk, L0_gnn_Wv, L0_gnn_Wo):
    import numpy as np
    import concourse.bacc as bacc
    from concourse.bass_utils import run_bass_kernel_spmd

    nc = bacc.Bacc("TRN2", target_bir_lowering=False, num_devices=1)
    arrays = {"in_x": x, "in_adj": adj, "in_wq": L0_gnn_Wq, "in_wk": L0_gnn_Wk, "in_wv": L0_gnn_Wv, "in_wo": L0_gnn_Wo}
    for name in ("in_wq", "in_wk"):
        arrays[name] = np.asarray(arrays[name]).reshape(D, G, HG, DK).transpose(0, 1, 3, 2).reshape(D, D)
    arrays = {name: np.ascontiguousarray(a) for name, a in arrays.items()}
    ins = [nc.dram_tensor(name, a.shape, mybir.dt.from_np(a.dtype), kind="ExternalInput").ap()
           for name, a in arrays.items()]
    out = nc.dram_tensor("out", (B, N, D), F32, kind="ExternalOutput").ap()
    graph_attention(nc, *ins, out)
    result = run_bass_kernel_spmd(nc, [arrays], core_ids=[0])
    return result.results[0]["out"]
```
